# Optimizing a Trainium2 kernel written in Bass

```python
import numpy as np
import jax
import jax.numpy as jnp

def _softmax(x, axis=-1):
    return jax.nn.softmax(x, axis=axis)

def _gelu(x):
    return jax.nn.gelu(x, approximate=True)

def _silu(x):
    return jax.nn.silu(x)

def _sigmoid(x):
    return jax.nn.sigmoid(x)

def _layernorm(x, axis=-1, eps=1e-05):
    m = jnp.mean(x, axis=axis, keepdims=True)
    v = jnp.var(x, axis=axis, keepdims=True)
    return (x - m) / jnp.sqrt(v + eps)

def _scatter_add(tgt, idx, src, axis=0):
    return tgt.at[idx].add(src)

def _segment_sum(src, seg, n):
    return jax.ops.segment_sum(src, seg, n)
kernel_name = 'mk_dlrm_tower_d1_rec_r8_eb6332'

def setup_inputs(seed: int=0):
    np.random.seed(seed)
    _w = jnp.asarray

    def _rec_inputs():
        import jax
        import jax.numpy as jnp
        _tk = jax.random.key(seed)
        dense_ctx = jax.random.normal(jax.random.fold_in(_tk, 190), (2048, 16), jnp.float32)
        ids = jnp.stack([jax.random.randint(jax.random.fold_in(_tk, 200 + f), (2048,), 0, v, jnp.int32) for f, v in enumerate([1250, 1000, 1250, 12500, 1250, 1250, 125000, 125000, 1250, 125000, 1250, 1250, 12500, 1000, 12500, 1250, 12500, 12500, 1000, 12500, 1250, 1000, 1250, 12500, 1250, 1000, 1250, 1250, 1000, 1250, 1000, 1000])], axis=1)
        tbl_0 = 0.05 * jax.random.normal(jax.random.fold_in(_tk, 500 + 0), (1250, 64), jnp.float32)
        tbl_1 = 0.05 * jax.random.normal(jax.random.fold_in(_tk, 500 + 1), (1000, 64), jnp.float32)
        tbl_2 = 0.05 * jax.random.normal(jax.random.fold_in(_tk, 500 + 2), (1250, 64), jnp.float32)
        tbl_3 = 0.05 * jax.random.normal(jax.random.fold_in(_tk, 500 + 3), (12500, 64), jnp.float32)
        tbl_4 = 0.05 * jax.random.normal(jax.random.fold_in(_tk, 500 + 4), (1250, 64), jnp.float32)
        tbl_5 = 0.05 * jax.random.normal(jax.random.fold_in(_tk, 500 + 5), (1250, 64), jnp.float32)
        tbl_6 = 0.05 * jax.random.normal(jax.random.fold_in(_tk, 500 + 6), (125000, 64), jnp.float32)
        tbl_7 = 0.05 * jax.random.normal(jax.random.fold_in(_tk, 500 + 7), (125000, 64), jnp.float32)
        tbl_8 = 0.05 * jax.random.normal(jax.random.fold_in(_tk, 500 + 8), (1250, 64), jnp.float32)
        tbl_9 = 0.05 * jax.random.normal(jax.random.fold_in(_tk, 500 + 9), (125000, 64), jnp.float32)
        tbl_10 = 0.05 * jax.random.normal(jax.random.fold_in(_tk, 500 + 10), (1250, 64), jnp.float32)
        tbl_11 = 0.05 * jax.random.normal(jax.random.fold_in(_tk, 500 + 11), (1250, 64), jnp.float32)
        tbl_12 = 0.05 * jax.random.normal(jax.random.fold_in(_tk, 500 + 12), (12500, 64), jnp.float32)
        tbl_13 = 0.05 * jax.random.normal(jax.random.fold_in(_tk, 500 + 13), (1000, 64), jnp.float32)
        tbl_14 = 0.05 * jax.random.normal(jax.random.fold_in(_tk, 500 + 14), (12500, 64), jnp.float32)
        tbl_15 = 0.05 * jax.random.normal(jax.random.fold_in(_tk, 500 + 15), (1250, 64), jnp.float32)
        tbl_16 = 0.05 * jax.random.normal(jax.random.fold_in(_tk, 500 + 16), (12500, 64), jnp.float32)
        tbl_17 = 0.05 * jax.random.normal(jax.random.fold_in(_tk, 500 + 17), (12500, 64), jnp.float32)
        tbl_18 = 0.05 * jax.random.normal(jax.random.fold_in(_tk, 500 + 18), (1000, 64), jnp.float32)
        tbl_19 = 0.05 * jax.random.normal(jax.random.fold_in(_tk, 500 + 19), (12500, 64), jnp.float32)
        tbl_20 = 0.05 * jax.random.normal(jax.random.fold_in(_tk, 500 + 20), (1250, 64), jnp.float32)
        tbl_21 = 0.05 * jax.random.normal(jax.random.fold_in(_tk, 500 + 21), (1000, 64), jnp.float32)
        tbl_22 = 0.05 * jax.random.normal(jax.random.fold_in(_tk, 500 + 22), (1250, 64), jnp.float32)
        tbl_23 = 0.05 * jax.random.normal(jax.random.fold_in(_tk, 500 + 23), (12500, 64), jnp.float32)
        tbl_24 = 0.05 * jax.random.normal(jax.random.fold_in(_tk, 500 + 24), (1250, 64), jnp.float32)
        tbl_25 = 0.05 * jax.random.normal(jax.random.fold_in(_tk, 500 + 25), (1000, 64), jnp.float32)
        tbl_26 = 0.05 * jax.random.normal(jax.random.fold_in(_tk, 500 + 26), (1250, 64), jnp.float32)
        tbl_27 = 0.05 * jax.random.normal(jax.random.fold_in(_tk, 500 + 27), (1250, 64), jnp.float32)
        tbl_28 = 0.05 * jax.random.normal(jax.random.fold_in(_tk, 500 + 28), (1000, 64), jnp.float32)
        tbl_29 = 0.05 * jax.random.normal(jax.random.fold_in(_tk, 500 + 29), (1250, 64), jnp.float32)
        tbl_30 = 0.05 * jax.random.normal(jax.random.fold_in(_tk, 500 + 30), (1000, 64), jnp.float32)
        tbl_31 = 0.05 * jax.random.normal(jax.random.fold_in(_tk, 500 + 31), (1000, 64), jnp.float32)
        _rk = jax.random.fold_in(_tk, 7)
        W_top1 = 0.0441942 * jax.random.normal(jax.random.fold_in(_tk, 801), (512, 512), jnp.float32)
        W_top2 = 0.0441942 * jax.random.normal(jax.random.fold_in(_tk, 802), (512, 256), jnp.float32)
        W_top3 = 0.0625 * jax.random.normal(jax.random.fold_in(_tk, 803), (256, 1), jnp.float32)
        b_top1 = jnp.zeros((512,), jnp.float32)
        b_top2 = jnp.zeros((256,), jnp.float32)
        return (dense_ctx, ids, tbl_0, tbl_1, tbl_2, tbl_3, tbl_4, tbl_5, tbl_6, tbl_7, tbl_8, tbl_9, tbl_10, tbl_11, tbl_12, tbl_13, tbl_14, tbl_15, tbl_16, tbl_17, tbl_18, tbl_19, tbl_20, tbl_21, tbl_22, tbl_23, tbl_24, tbl_25, tbl_26, tbl_27, tbl_28, tbl_29, tbl_30, tbl_31, W_top1, b_top1, W_top2, b_top2, W_top3)
    dense_ctx, ids, tbl_0, tbl_1, tbl_2, tbl_3, tbl_4, tbl_5, tbl_6, tbl_7, tbl_8, tbl_9, tbl_10, tbl_11, tbl_12, tbl_13, tbl_14, tbl_15, tbl_16, tbl_17, tbl_18, tbl_19, tbl_20, tbl_21, tbl_22, tbl_23, tbl_24, tbl_25, tbl_26, tbl_27, tbl_28, tbl_29, tbl_30, tbl_31, W_top1, b_top1, W_top2, b_top2, W_top3 = _rec_inputs()

    def _L0_rec_setup():
        import jax, jax.numpy as jnp
        import numpy as np
        key = jax.random.key(seed)
        k1, k2 = jax.random.split(key)
        B, F, D = (512, 32, 64)
        P = F * (F - 1) // 2
        x = jax.random.normal(k1, (B, F, D), dtype=jnp.float32)
        W = jax.random.normal(k2, (P, D, D), dtype=jnp.float32) * (1.0 / np.sqrt(D))
        return {'x': x, 'W': W}
    _L0_rec_all = _L0_rec_setup()
    _L0_rec_in = {k: v for k, v in _L0_rec_all.items() if k in ('W',)}
    del _L0_rec_all
    return {'dense_ctx': dense_ctx, 'ids': ids, 'tbl_0': tbl_0, 'tbl_1': tbl_1, 'tbl_2': tbl_2, 'tbl_3': tbl_3, 'tbl_4': tbl_4, 'tbl_5': tbl_5, 'tbl_6': tbl_6, 'tbl_7': tbl_7, 'tbl_8': tbl_8, 'tbl_9': tbl_9, 'tbl_10': tbl_10, 'tbl_11': tbl_11, 'tbl_12': tbl_12, 'tbl_13': tbl_13, 'tbl_14': tbl_14, 'tbl_15': tbl_15, 'tbl_16': tbl_16, 'tbl_17': tbl_17, 'tbl_18': tbl_18, 'tbl_19': tbl_19, 'tbl_20': tbl_20, 'tbl_21': tbl_21, 'tbl_22': tbl_22, 'tbl_23': tbl_23, 'tbl_24': tbl_24, 'tbl_25': tbl_25, 'tbl_26': tbl_26, 'tbl_27': tbl_27, 'tbl_28': tbl_28, 'tbl_29': tbl_29, 'tbl_30': tbl_30, 'tbl_31': tbl_31, 'W_top1': W_top1, 'b_top1': b_top1, 'W_top2': W_top2, 'b_top2': b_top2, 'W_top3': W_top3, 'L0_rec_W': _L0_rec_in['W']}

def reference(dense_ctx, ids, tbl_0, tbl_1, tbl_2, tbl_3, tbl_4, tbl_5, tbl_6, tbl_7, tbl_8, tbl_9, tbl_10, tbl_11, tbl_12, tbl_13, tbl_14, tbl_15, tbl_16, tbl_17, tbl_18, tbl_19, tbl_20, tbl_21, tbl_22, tbl_23, tbl_24, tbl_25, tbl_26, tbl_27, tbl_28, tbl_29, tbl_30, tbl_31, W_top1, b_top1, W_top2, b_top2, W_top3, L0_rec_W):
    import jax
    import jax.numpy as jnp

    def _L0_rec_ref(x, W):
        import jax, jax.numpy as jnp
        import numpy as np
        F = x.shape[1]
        idx_i, idx_j = np.triu_indices(F, k=1)
        xi = x[:, idx_i, :]
        xj = x[:, idx_j, :]
        left = jnp.einsum('bpd,pde->bpe', xi, W)
        out = jnp.sum(left * xj, axis=-1)
        return out
    e = jnp.stack([tbl_0[ids[:, 0]], tbl_1[ids[:, 1]], tbl_2[ids[:, 2]], tbl_3[ids[:, 3]], tbl_4[ids[:, 4]], tbl_5[ids[:, 5]], tbl_6[ids[:, 6]], tbl_7[ids[:, 7]], tbl_8[ids[:, 8]], tbl_9[ids[:, 9]], tbl_10[ids[:, 10]], tbl_11[ids[:, 11]], tbl_12[ids[:, 12]], tbl_13[ids[:, 13]], tbl_14[ids[:, 14]], tbl_15[ids[:, 15]], tbl_16[ids[:, 16]], tbl_17[ids[:, 17]], tbl_18[ids[:, 18]], tbl_19[ids[:, 19]], tbl_20[ids[:, 20]], tbl_21[ids[:, 21]], tbl_22[ids[:, 22]], tbl_23[ids[:, 23]], tbl_24[ids[:, 24]], tbl_25[ids[:, 25]], tbl_26[ids[:, 26]], tbl_27[ids[:, 27]], tbl_28[ids[:, 28]], tbl_29[ids[:, 29]], tbl_30[ids[:, 30]], tbl_31[ids[:, 31]]], axis=1)
    z = _L0_rec_ref(e, L0_rec_W)
    z = z.reshape(z.shape[0], -1)
    h = jnp.concatenate([z, dense_ctx], axis=1)
    h = jnp.maximum(h @ W_top1 + b_top1, 0.0)
    h = jnp.maximum(h @ W_top2 + b_top2, 0.0)
    y = h @ W_top3
    return y

_drawn_inputs = setup_inputs


def setup_inputs(seed=0):
    import zlib

    import numpy as np

    out = dict(_drawn_inputs(seed))
    spreads = {'b_top1': (0.0, 0.1), 'b_top2': (0.0, 0.1)}
    factors = {}
    for name, (base, spread) in spreads.items():
        noise = np.random.default_rng([zlib.crc32(name.encode()), seed]).standard_normal(out[name].shape)
        drawn = base * np.exp(spread * noise) if base else spread * noise
        out[name] = jnp.asarray(drawn.astype(out[name].dtype))
    for name, factor in factors.items():
        out[name] = (out[name] * factor).astype(out[name].dtype)
    return out
```

```python
from contextlib import ExitStack

import concourse.bass as bass
import concourse.mybir as mybir
import numpy as np

F32 = mybir.dt.float32
F32R = mybir.dt.float32r
I32 = mybir.dt.int32
ALU = mybir.AluOpType
ACT = mybir.ActivationFunctionType

F, D, P = 32, 64, 128
BATCH, BLK = 2048, 512
NBLK = BATCH // BLK
TB = BLK // P
DUO = 2 * D

GROUPS = list(range(F - 2, -1, -1))
DUOS = [(i, m) for i in GROUPS for m in range((i + 1) // 2, F // 2)]
NDUO = len(DUOS)
NUNIT = NDUO // 2
NQUAD = NDUO // 4
QCH = 16
NCH = NQUAD // QCH
NGRP = len(GROUPS)
FIRST = {i: next(d for d, (g, _) in enumerate(DUOS) if g == i) for i in GROUPS}
LAST = {i: max(d for d, (g, _) in enumerate(DUOS) if g == i) for i in GROUPS}

NRAW = 4
NWRAW = 2
NPROD = 4
NLEFT = 2
LAG = 2


def pair_index(i, j):
    return i * F - i * (i + 1) // 2 + (j - i - 1)


def halves(d):
    i, m = DUOS[d]
    return [pair_index(i, j) if j > i else None for j in (2 * m, 2 * m + 1)]


EMPTY = [d for d in range(NDUO) if halves(d)[0] is None]


def quad_runs(n):
    runs = []
    for c, p in enumerate(h for d in range(4 * n, 4 * n + 4) for h in halves(d)):
        if p is None:
            continue
        if runs and runs[-1][0] + runs[-1][2] == c and runs[-1][1] + runs[-1][2] == p:
            runs[-1][2] += 1
        else:
            runs.append([c, p, 1])
    return [(c * D, p, k) for c, p, k in runs]


def quad_spans(n):
    spans = []
    for c, _, k in quad_runs(n):
        if spans and spans[-1][1] == c:
            spans[-1][1] = c + k * D
        else:
            spans.append([c, c + k * D])
    return spans


def z_row(d):
    return d // (4 * QCH), 32 * (d % 4) + 2 * (d // 4 % QCH)


def block_steps():
    steps = [("twin", F // 2 - 1), ("f", F - 2), ("x", F // 2 - 1), ("twin", F // 2 - 2)]
    n = 0
    for i in GROUPS:
        if i > 0:
            if (i - 1) % 2 == 0:
                steps.append(("x", (i - 1) // 2))
            steps.append(("f", i - 1))
            if (i - 1) % 2 == 0 and i > 1 and i < F - 1:
                steps.append(("twin", (i - 1) // 2 - 1))
        for d in range(FIRST[i], LAST[i] + 1):
            steps.append(("left", d))
            if d == 4 * n + 3 + LAG:
                steps.append(("sum", n))
                n += 1
    return steps + [("sum", k) for k in range(n, NQUAD)]


def wait(engine, semaphore, value):
    if not isinstance(value, int) or value > 0:
        engine.wait_ge(semaphore, value)


STEPS = block_steps()
F_COUNT = {i: F - 1 - i for i in GROUPS}
X_COUNT = {m: F // 2 - m for m in range(F // 2)}


def interactions(nc, ids, tables, w_pair, w_top1, z_dram, w1_dram):
    with ExitStack() as ctx:
        sb = lambda name, shape, dt=F32: ctx.enter_context(nc.sbuf_tensor(name, shape, dt))
        ps = lambda name, shape: ctx.enter_context(nc.psum_tensor(name, shape, F32))
        sem = lambda name: ctx.enter_context(nc.semaphore(name))

        w_split = sb("w_split", [P, NDUO, DUO], F32R)
        w_raw = sb("w_raw", [P, NWRAW, 4 * DUO])
        xT = sb("xT", [P, F // 2, BLK])
        x_split = sb("x_split", [P, 2, 2, BLK], F32R)
        rows = sb("rows", [P, NRAW, TB, 4, D])
        prod = sb("prod", [P, NPROD, 2, BLK])
        z_out = sb("z_out", [P, BLK])
        ids_now = sb("ids_now", [P, TB, F], I32)
        ident = sb("ident", [P, P])
        pick = sb("pick", [P, 64])

        left = ps("left", [P, 2 * NLEFT, BLK])
        z_ps = ps("z_ps", [P, BLK])
        f_ps = ps("f_ps", [P, 2, BLK])
        x_ps = ps("x_ps", [P, BLK])

        ids_loaded = sem("ids_loaded")
        const_set = sem("const_set")
        consts = sem("consts")
        w_zeroed = sem("w_zeroed")
        rows_loaded = [sem(f"rows_loaded{r}") for r in range(NRAW)]
        w_loaded = [sem(f"w_loaded{r}") for r in range(NWRAW)]
        w_hi = sem("w_hi")
        w_ready = sem("w_ready")
        pairs_begun = sem("pairs_begun")
        twinned = sem("twinned")
        f_in_psum = sem("f_in_psum")
        x_in_psum = sem("x_in_psum")
        f_hi = sem("f_hi")
        f_ready = sem("f_ready")
        x_ready = sem("x_ready")
        left_done = sem("left_done")
        prod_ready = sem("prod_ready")
        sum_done = sem("sum_done")
        z_copied = sem("z_copied")
        z_stored = sem("z_stored")
        w1_moved = sem("w1_moved")

        block = ctx.enter_context(nc.Block())

        @block.sync
        def _(sp):
            def store_z(b, c):
                sp.wait_ge(z_copied, NCH * b + c + 1)
                sp.dma_start(z_dram[b, :, c, :], z_out[:, :]).then_inc(z_stored, 16)

            for n in range(NQUAD):
                if n >= NWRAW:
                    sp.wait_ge(w_ready, n - NWRAW + 1)
                for c, p, k in quad_runs(n):
                    for half in (0, D):
                        sp.dma_start(w_raw[half:half + D, n % NWRAW, c:c + k * D].rearrange("d (p e) -> d p e", e=D),
                                     w_pair[p:p + k, :, :].rearrange("p d e -> d p e")).then_inc(w_loaded[n % NWRAW], 16)
                if n % QCH == 8 and n > QCH:
                    store_z(0, n // QCH - 1)
            store_z(0, NCH - 1)

            sp.wait_ge(w_zeroed, 1)
            zeros = w_split[0:8, EMPTY[0], 0:D].bitcast(F32)
            for c in range(NCH):
                for d in range(4 * QCH * c, 4 * QCH * (c + 1)):
                    _, r = z_row(d)
                    lower, upper = halves(d)
                    if lower is None:
                        sp.dma_start(w1_dram[r, c, :].rearrange("(a n) -> a n", n=D), zeros).then_inc(w1_moved, 16)
                        sp.dma_start(w1_dram[r + 1:r + 2, c, :], w_top1[upper:upper + 1, :]).then_inc(w1_moved, 16)
                    else:
                        sp.dma_start(w1_dram[r:r + 2, c, :], w_top1[lower:lower + 2, :]).then_inc(w1_moved, 16)
                store_z(1, c)
            with sp.Fori(2, NBLK) as b:
                for c in range(NCH):
                    store_z(b, c)
            sp.wait_ge(z_stored, 16 * NCH * NBLK)
            sp.wait_ge(w1_moved, 16 * (NDUO + F // 2))

        @block.gpsimd
        def _(pool):
            nc.gpsimd.memset(ident[:, :], 0.0).then_inc(const_set, 1)
            nc.gpsimd.memset(pick[:, :], 0.0).then_inc(const_set, 1)
            pool.wait_ge(const_set, 2)
            nc.gpsimd.affine_select(out=ident[:, :], in_=ident[:, :], compare_op=ALU.not_equal, fill=1.0,
                                    base=0, pattern=[[-1, P]], channel_multiplier=1).then_inc(consts, 1)
            pool.wait_ge(consts, 1)
            nc.gpsimd.memset(pick[0:D, 30:31], 1.0).then_inc(consts, 1)
            pool.wait_ge(consts, 2)
            nc.gpsimd.memset(pick[D:P, 31:32], 1.0).then_inc(consts, 1)
            ids_v = ids.rearrange("(t p) f -> p t f", p=P)
            def body(b):
                for r in range(NRAW):
                    wait(pool, rows_loaded[r], 16 * 2 * TB * (F // 2 // NRAW) * b)
                pool.dma_start(ids_now[:, :, :], ids_v[:, bass.ds(b * TB, TB), :]).then_inc(ids_loaded, 16)
                pool.wait_ge(ids_loaded, 16 * b + 16)
                for s in range(F // 2):
                    m = F // 2 - 1 - s
                    r = s % NRAW
                    before = 2 * (s - NRAW) + 1 if s >= NRAW else 2 * (s - NRAW + F // 2) + 1 - NGRP
                    wait(pool, f_in_psum, NGRP * b + before)
                    pool.sem_inc(pairs_begun, 1)
                    for f in (2 * m + 1, 2 * m):
                        for t in range(TB):
                            pool.indirect_dma_start(
                                rows[:, r, t, 3 * (f % 2), :], None, tables[f],
                                bass.IndirectOffsetOnAxis(ap=ids_now[:, t, f:f + 1], axis=0),
                            ).then_inc(rows_loaded[r], 16)

            body(0)
            with pool.Fori(1, NBLK) as b:
                body(b)

        @block.scalar
        def _(act):
            def split_w(n):
                loads = sum(2 * len(quad_runs(k)) for k in range(n % NWRAW, n + 1, NWRAW))
                act.wait_ge(w_loaded[n % NWRAW], 16 * loads)
                flat = w_split[:, 4 * n:4 * n + 4, :].rearrange("p d c -> p (d c)")
                for a, e in quad_spans(n):
                    last = nc.scalar.activation(flat[:, a:e], w_raw[:, n % NWRAW, a:e], ACT.Copy)
                last.then_inc(w_hi, 1)

            def body(b, with_w):
                w_next = 0
                for kind, v in STEPS:
                    if with_w and kind == "left" and v % 4 == 0:
                        while w_next < min(NQUAD, v // 4 + 3):
                            split_w(w_next)
                            w_next += 1
                    if kind == "twin":
                        s = F // 2 - 1 - v
                        wait(act, rows_loaded[s % NRAW], 16 * 2 * TB * (F // 2 // NRAW * b + s // NRAW + 1))
                        nc.scalar.activation(rows[:, s % NRAW, :, 1:3, :], rows[:, s % NRAW, :, 0:4:3, :],
                                             ACT.Copy).then_inc(twinned, 1)
                    if kind == "f":
                        wait(act, f_in_psum, NGRP * b + F_COUNT[v])
                        wait(act, left_done, NDUO * b + (LAST[v + 2] + 1 if v + 2 in LAST else 0))
                        nc.scalar.activation(x_split[:, v % 2, 0, :], f_ps[:, v % 2, :], ACT.Copy).then_inc(f_hi, 1)
                    if kind == "x":
                        wait(act, x_in_psum, F // 2 * b + X_COUNT[v])
                        wait(act, prod_ready, NUNIT * b)
                        nc.scalar.activation(xT[:, v, :], x_ps[:, :], ACT.Copy).then_inc(x_ready, 1)
                    if kind == "sum" and v % QCH == QCH - 1:
                        c = v // QCH
                        wait(act, sum_done, NQUAD * b + v + 1)
                        wait(act, z_stored, 16 * (NCH * b + c))
                        nc.scalar.activation(z_out[:, :], z_ps[:, :], ACT.Copy).then_inc(z_copied, 1)

            body(0, True)
            with act.Fori(1, NBLK) as b:
                body(b, False)

        @block.vector
        def _(dve):
            for d in EMPTY:
                last = nc.vector.memset(w_split[:, d, 0:D].bitcast(F32), 0.0)
            last.then_inc(w_zeroed, 1)

            def split_w(n):
                dve.wait_ge(w_hi, n + 1)
                flat = w_split[:, 4 * n:4 * n + 4, :].rearrange("p d c -> p (d c)")
                for a, e in quad_spans(n):
                    last = nc.vector.tensor_tensor(flat[D:P, a:e], w_raw[D:P, n % NWRAW, a:e], flat[D:P, a:e], ALU.subtract)
                last.then_inc(w_ready, 1)

            def body(b, with_w):
                w_next = 0
                for kind, v in STEPS:
                    if with_w and kind == "left" and v % 4 == 0:
                        while w_next < min(NQUAD, v // 4 + 3):
                            split_w(w_next)
                            w_next += 1
                    if kind == "f":
                        wait(dve, f_hi, NGRP * b + F_COUNT[v])
                        nc.vector.tensor_tensor(x_split[:, v % 2, 1, :], f_ps[:, v % 2, :], x_split[:, v % 2, 0, :],
                                                ALU.subtract).then_inc(f_ready, 1)
                    if kind == "left" and v % 2 == 1:
                        u = v // 2
                        m0, m1 = DUOS[v - 1][1], DUOS[v][1]
                        wait(dve, left_done, NDUO * b + v + 1)
                        wait(dve, x_ready, F // 2 * b + X_COUNT[min(m0, m1)])
                        wait(dve, sum_done, NQUAD * b + max(0, (u - NPROD) // 2 + 1))
                        if m0 == m1:
                            other = xT[:, m0:m0 + 1, :].to_broadcast([P, 2, BLK])
                        else:
                            step = m1 - m0
                            other = xT[:, m0:m1 + 1:step, :] if step > 0 else xT[:, m0:m1 - 1 if m1 else None:step, :]
                        nc.vector.tensor_tensor(prod[:, u % NPROD, :, :], left[:, 2 * (u % NLEFT):2 * (u % NLEFT) + 2, :],
                                                other, ALU.mult).then_inc(prod_ready, 1)

            body(0, True)
            with dve.Fori(1, NBLK) as b:
                body(b, False)

        @block.tensor
        def _(pe):
            pe.wait_ge(consts, 3)
            def body(b):
                for kind, v in STEPS:
                    if kind in "fx":
                        m = v // 2 if kind == "f" else v
                        r = (F // 2 - 1 - m) % NRAW
                        wait(pe, twinned, F // 2 * b + F // 2 - m)
                    if kind == "f":
                        wait(pe, f_ready, NGRP * b + max(0, F_COUNT[v] - 2))
                        for t in range(TB):
                            twice = rows[:, r, t, 2 * (v % 2):2 * (v % 2) + 2, :].rearrange("p f d -> p (f d)")
                            last = nc.tensor.transpose(f_ps[:, v % 2, t * P:(t + 1) * P], twice, ident[:, :])
                        last.then_inc(f_in_psum, 1)
                    if kind == "x":
                        wait(pe, x_ready, F // 2 * b + X_COUNT[v] - 1)
                        for t in range(TB):
                            both = rows[:, r, t, 1:3, :].rearrange("p f d -> p (f d)")
                            last = nc.tensor.transpose(x_ps[:, t * P:(t + 1) * P], both, ident[:, :])
                        last.then_inc(x_in_psum, 1)
                    if kind == "left":
                        i, u = DUOS[v][0], v // 2
                        if v == FIRST[i]:
                            wait(pe, f_ready, NGRP * b + F_COUNT[i])
                        if v % 4 == 0:
                            pe.wait_ge(w_ready, v // 4 + 1)
                        if v % 2 == 0:
                            wait(pe, prod_ready, NUNIT * b + max(0, u - NLEFT + 1))
                        for part in range(2):
                            last = nc.tensor.matmul(left[:, v % (2 * NLEFT), :], w_split[:, v, :],
                                                    x_split[:, i % 2, part, :], start=part == 0, stop=part == 1)
                        last.then_inc(left_done, 1)
                    if kind == "sum":
                        wait(pe, prod_ready, NUNIT * b + 2 * v + 2)
                        k = v % QCH
                        if k == 0:
                            wait(pe, z_copied, NCH * b + v // QCH)
                        for t in range(4):
                            last = nc.tensor.matmul(z_ps[32 * t:32 * t + 32, :], pick[:, 30 - 2 * k:62 - 2 * k],
                                                    prod[:, (2 * v + t // 2) % NPROD, t % 2, :],
                                                    start=k == 0, stop=k == QCH - 1)
                        last.then_inc(sum_done, 1)

            body(0)
            with pe.Fori(1, NBLK) as b:
                body(b)


def top(nc, z_dram, w1_dram, dense, w_top1, b_top1, w_top2, b_top2, w_top3, y):
    H1, H2 = w_top2.shape
    ND = dense.shape[1]
    K1, K2 = H1 // P, H2 // P
    NPAIR = w_top1.shape[0] - ND
    with ExitStack() as ctx:
        sb = lambda name, shape, dt=F32: ctx.enter_context(nc.sbuf_tensor(name, shape, dt))
        ps = lambda name, shape: ctx.enter_context(nc.psum_tensor(name, shape, F32))
        sem = lambda name: ctx.enter_context(nc.semaphore(name))

        w1 = sb("w1", [P, NCH, H1])
        w1d = sb("w1d", [ND, H1])
        w2 = sb("w2", [P, K1, H2])
        w3 = sb("w3", [P, K2])
        b1 = sb("b1", [P, K1])
        b2 = sb("b2", [P, K2])
        ident2 = sb("ident2", [P, P])
        zT = sb("zT", [P, NBLK, NCH, BLK])
        dense_sb = sb("dense_sb", [P, BATCH // P, ND])
        denseT = sb("denseT", [ND, BATCH])
        h1T = sb("h1T", [P, 2, K1, BLK])
        h2T = sb("h2T", [P, 2, K2, BLK])
        y_sb = sb("y_sb", [1, BATCH])

        d_ps = ps("d_ps", [ND, BLK])
        h1_ps = ps("h1_ps", [P, 2, BLK])
        h2_ps = ps("h2_ps", [P, 2, BLK])
        y_ps = ps("y_ps", [1, BLK])

        w_in = sem("w_in")
        z_in = [sem(f"z_in{b}") for b in range(NBLK)]
        dense_in = sem("dense_in")
        id_zero = sem("id_zero")
        id_set = sem("id_set")
        d_in_psum = sem("d_in_psum")
        d_ready = sem("d_ready")
        h1_in_psum = sem("h1_in_psum")
        h1_ready = sem("h1_ready")
        h2_in_psum = sem("h2_in_psum")
        h2_ready = sem("h2_ready")
        y_in_psum = sem("y_in_psum")
        y_ready = sem("y_ready")
        y_out = sem("y_out")
        N_W = 6

        block = ctx.enter_context(nc.Block())

        @block.sync
        def _(sp):
            sp.dma_start(dense_sb[:, :, :], dense.rearrange("(t p) k -> p t k", p=P)).then_inc(dense_in, 16)
            sp.dma_start(zT[:, 0, :, :], z_dram[0, :, :, :]).then_inc(z_in[0], 16)
            sp.dma_start(w1[:, :, :], w1_dram[:, :, :]).then_inc(w_in, 16)
            sp.dma_start(w1d[:, :], w_top1[NPAIR:NPAIR + ND, :]).then_inc(w_in, 16)
            sp.dma_start(b1[:, :], b_top1.rearrange("(k p) -> p k", p=P), allow_slow_non_contiguous=True).then_inc(w_in, 16)
            sp.dma_start(b2[:, :], b_top2.rearrange("(k p) -> p k", p=P), allow_slow_non_contiguous=True).then_inc(w_in, 16)
            sp.dma_start(w3[:, :], w_top3.rearrange("(k p) o -> p (k o)", p=P), allow_slow_non_contiguous=True).then_inc(w_in, 16)
            sp.dma_start(w2[:, :, :], w_top2.rearrange("(k p) n -> p k n", p=P)).then_inc(w_in, 16)
            for b in range(1, NBLK):
                sp.dma_start(zT[:, b, :, :], z_dram[b, :, :, :]).then_inc(z_in[b], 16)
            sp.wait_ge(y_ready, NBLK)
            sp.dma_start(y.rearrange("b o -> o b"), y_sb[:, :]).then_inc(y_out, 16)
            sp.wait_ge(y_out, 16)

        @block.gpsimd
        def _(pool):
            nc.gpsimd.memset(ident2[:, :], 0.0).then_inc(id_zero, 1)
            pool.wait_ge(id_zero, 1)
            nc.gpsimd.affine_select(out=ident2[:, :], in_=ident2[:, :], compare_op=ALU.not_equal, fill=1.0,
                                    base=0, pattern=[[-1, P]], channel_multiplier=1).then_inc(id_set, 1)

        @block.tensor
        def _(pe):
            pe.wait_ge(id_set, 1)
            pe.wait_ge(dense_in, 16)
            for b in range(NBLK):
                if b:
                    pe.wait_ge(d_ready, b)
                for t in range(TB):
                    last = nc.tensor.transpose(d_ps[:, t * P:(t + 1) * P], dense_sb[:, TB * b + t, :], ident2[:, :])
                last.then_inc(d_in_psum, 1)
            pe.wait_ge(w_in, 16 * N_W)
            pe.wait_ge(d_ready, NBLK)
            for b in range(NBLK):
                pe.wait_ge(z_in[b], 16)
                for q in range(K1):
                    n = K1 * b + q
                    if n >= 2:
                        pe.wait_ge(h1_ready, n - 1)
                    for c in range(NCH):
                        nc.tensor.matmul(h1_ps[:, n % 2, :], w1[:, c, q * P:(q + 1) * P], zT[:, b, c, :],
                                         start=c == 0, stop=False)
                    nc.tensor.matmul(h1_ps[:, n % 2, :], w1d[:, q * P:(q + 1) * P], denseT[:, b * BLK:(b + 1) * BLK],
                                     start=False, stop=True).then_inc(h1_in_psum, 1)
                pe.wait_ge(h1_ready, K1 * (b + 1))
                for q in range(K2):
                    n = K2 * b + q
                    if n >= 2:
                        pe.wait_ge(h2_ready, n - 1)
                    for c in range(K1):
                        last = nc.tensor.matmul(h2_ps[:, n % 2, :], w2[:, c, q * P:(q + 1) * P], h1T[:, b % 2, c, :],
                                                start=c == 0, stop=c == K1 - 1)
                    last.then_inc(h2_in_psum, 1)
                pe.wait_ge(h2_ready, K2 * (b + 1))
                if b:
                    pe.wait_ge(y_ready, b)
                for c in range(K2):
                    last = nc.tensor.matmul(y_ps[:, :], w3[:, c:c + 1], h2T[:, b % 2, c, :], start=c == 0, stop=c == K2 - 1)
                last.then_inc(y_in_psum, 1)

        @block.scalar
        def _(act):
            for b in range(NBLK):
                act.wait_ge(d_in_psum, b + 1)
                nc.scalar.activation(denseT[:, b * BLK:(b + 1) * BLK], d_ps[:, :], ACT.Copy).then_inc(d_ready, 1)
            act.wait_ge(w_in, 16 * N_W)
            for b in range(NBLK):
                for q in range(K1):
                    act.wait_ge(h1_in_psum, K1 * b + q + 1)
                    if b >= 2:
                        act.wait_ge(h2_in_psum, K2 * (b - 1))
                    nc.scalar.activation(h1T[:, b % 2, q, :], h1_ps[:, (K1 * b + q) % 2, :], ACT.Relu,
                                         bias=b1[:, q:q + 1]).then_inc(h1_ready, 1)
                for q in range(K2):
                    act.wait_ge(h2_in_psum, K2 * b + q + 1)
                    if b >= 2:
                        act.wait_ge(y_in_psum, b - 1)
                    nc.scalar.activation(h2T[:, b % 2, q, :], h2_ps[:, (K2 * b + q) % 2, :], ACT.Relu,
                                         bias=b2[:, q:q + 1]).then_inc(h2_ready, 1)
                act.wait_ge(y_in_psum, b + 1)
                nc.scalar.activation(y_sb[:, b * BLK:(b + 1) * BLK], y_ps[:, :], ACT.Copy).then_inc(y_ready, 1)


def build(nc, t):
    z_dram = nc.dram_tensor("z_dram", (NBLK, P, NCH, BLK), F32, kind="Internal").ap()
    w1_dram = nc.dram_tensor("w1_dram", (P, NCH, t["W_top1"].shape[1]), F32, kind="Internal").ap()
    interactions(nc, t["ids"], [t[f"tbl_{f}"] for f in range(F)], t["L0_rec_W"], t["W_top1"], z_dram, w1_dram)
    top(nc, z_dram, w1_dram, t["dense_ctx"], t["W_top1"], t["b_top1"], t["W_top2"], t["b_top2"], t["W_top3"], t["y"])


def kernel(**inputs):
    import concourse.bacc as bacc
    from concourse.bass_utils import run_bass_kernel_spmd

    nc = bacc.Bacc("TRN2", target_bir_lowering=False, num_devices=1)
    arrays, tensors = {}, {}
    for name, value in inputs.items():
        a = np.ascontiguousarray(value)
        arrays[f"in_{name}"] = a
        tensors[name] = nc.dram_tensor(f"in_{name}", a.shape, mybir.dt.from_np(a.dtype), kind="ExternalInput").ap()
    tensors["y"] = nc.dram_tensor("out_y", (BATCH, 1), F32, kind="ExternalOutput").ap()
    build(nc, tensors)
    result = run_bass_kernel_spmd(nc, [arrays], core_ids=[0])
    return result.results[0]["out_y"]
```

```python
from contextlib import ExitStack

import concourse.bass as bass
import concourse.mybir as mybir
import numpy as np

F32 = mybir.dt.float32
F32R = mybir.dt.float32r
I32 = mybir.dt.int32
ALU = mybir.AluOpType
ACT = mybir.ActivationFunctionType

F, D, P = 32, 64, 128
BATCH, BLK = 2048, 512
NBLK = BATCH // BLK
TB = BLK // P
DUO = 2 * D
NPAIR = F * (F - 1) // 2
NM = F // 2

GROUPS = list(range(F - 2, -1, -1))
DUOS = [(i, m) for i in GROUPS for m in sorted(range((i + 1) // 2, NM), reverse=i == 0)]
NDUO = len(DUOS)
NUNIT = NDUO // 2
NQUAD = NDUO // 4
QCH = 16
NCH = NQUAD // QCH
NGRP = len(GROUPS)
FIRST = {i: next(d for d, (g, _) in enumerate(DUOS) if g == i) for i in GROUPS}
LAST = {i: max(d for d, (g, _) in enumerate(DUOS) if g == i) for i in GROUPS}
LAST_UNIT = {m: max(d for d, (_, k) in enumerate(DUOS) if k == m) // 2 for m in range(NM)}

NROWS = 4
NWRAW = 2
NPROD = 4
NLEFT = 3
NTWICE = 3
LAG = 4
W_AHEAD = 3
W_PART = 4 * QCH


def pair_index(i, j):
    return i * F - i * (i + 1) // 2 + (j - i - 1)


def halves(d):
    i, m = DUOS[d]
    return [pair_index(i, j) if j > i else None for j in (2 * m, 2 * m + 1)]


EMPTY = [d for d in range(NDUO) if halves(d)[0] is None]


def quad_runs(n):
    runs = []
    for c, p in enumerate(h for d in range(4 * n, 4 * n + 4) for h in halves(d)):
        if p is None:
            continue
        if runs and runs[-1][0] + runs[-1][2] == c and runs[-1][1] + runs[-1][2] == p:
            runs[-1][2] += 1
        else:
            runs.append([c, p, 1])
    return [(c * D, p, k) for c, p, k in runs]


def quad_spans(n):
    spans = []
    for c, _, k in quad_runs(n):
        if spans and spans[-1][1] == c:
            spans[-1][1] = c + k * D
        else:
            spans.append([c, c + k * D])
    return spans


def z_row(d):
    return d // (4 * QCH), 32 * (d % 4) + 2 * (d // 4 % QCH)


def twice_slots():
    slots, place = {}, 0
    for i in GROUPS:
        slots[i] = place % NTWICE
        place += 2 if i in (8, 5) else 1
    return slots


SLOT = twice_slots()


def before_in_ring(slots, order, x):
    at = order.index(x)
    for k in range(at - 1, at - 1 - len(order), -1):
        if slots[order[k]] == slots[x]:
            return (0 if k >= 0 else -1), order[k]


def block_steps():
    before = {d: [] for d in range(NDUO)}
    at = 0
    for i in GROUPS[2:]:
        _, user = before_in_ring(SLOT, GROUPS, i)
        free = FIRST[min(i + 2, F - 2)] if user != i + 2 else FIRST[i + 1]
        if i % 2 == 1:
            at_lo = min(at + 4, FIRST[i])
            before[at_lo].append(("lo", i // 2, 0))
            free = max(free, min(at_lo + 4, FIRST[i]))
        at = max(at, free)
        before[at].append(("f", i, 0))
        if i % 2 == 0 and i > 0:
            before[at].append(("x", i // 2 - 1, 0))
    for at, kind, v in ((4, "x", NM - 1), (6, "lo", NM - 1), (8, "f", F - 2), (8, "x", NM - 2),
                        (11, "lo", NM - 2), (13, "f", F - 3)):
        before[FIRST[0] + at].append((kind, v, 1))
    steps = []
    for d in range(NDUO):
        steps += before[d] + [("left", d, 0)]
        n, rest = divmod(d - 3 - LAG, 4)
        if rest == 0:
            steps.append(("sum", n % NQUAD, 0 if n >= 0 else -1))
    return steps


PROLOGUE = [("x", NM - 1, 0), ("lo", NM - 1, 0), ("f", F - 2, 0),
            ("x", NM - 2, 0), ("lo", NM - 2, 0), ("f", F - 3, 0)]
STEPS = block_steps()


def steps_of(first, last):
    steps = [s for s in STEPS if not (first and s[2] < 0) and not (last and s[2] > 0)]
    if last:
        steps += [(kind, v, 0) for kind, v, o in STEPS if o < 0]
    return (PROLOGUE if first else []) + steps


F_COUNT = {i: F - 1 - i for i in GROUPS}
X_COUNT = {m: NM - m for m in range(NM)}


def wait(engine, semaphore, value):
    if not isinstance(value, int) or value > 0:
        engine.wait_ge(semaphore, value)


def over_blocks(engine, body):
    body(0, True, False)
    with engine.Fori(1, NBLK - 1) as b:
        body(b, False, False)
    body(NBLK - 1, False, True)


def build(nc, t):
    H1, H2 = t["W_top2"].shape
    ND = t["dense_ctx"].shape[1]
    K1, K2 = H1 // P, H2 // P
    tables = [t[f"tbl_{f}"] for f in range(F)]
    w_top1 = t["W_top1"]
    z_dram = nc.dram_tensor("z_dram", (NBLK, P, NCH, BLK), F32, kind="Internal").ap()
    w1_dram = nc.dram_tensor("w1_dram", (P, NCH, H1), F32, kind="Internal").ap()

    with ExitStack() as ctx:
        sb = lambda name, shape, dt=F32: ctx.enter_context(nc.sbuf_tensor(name, shape, dt))
        ps = lambda name, shape: ctx.enter_context(nc.psum_tensor(name, shape, F32))
        sem = lambda name: ctx.enter_context(nc.semaphore(name))

        ident = sb("ident", [P, P])
        pick = sb("pick", [P, 64])
        w_raw = sb("w_raw", [P, NWRAW, 4 * DUO])
        xT = sb("xT", [P, NM, BLK])
        x_parts = sb("x_parts", [P, 2, BLK], F32R)
        x_twice = sb("x_twice", [P, NTWICE, 2, BLK], F32R)
        rows = sb("rows", [P, NROWS, TB, 2, D])
        prod = sb("prod", [P, NPROD, 2, BLK])
        z_out = sb("z_out", [P, BLK])
        ids_now = sb("ids_now", [P, TB, F], I32)

        with nc.sbuf_tensor("w_split_a", [P, W_PART, DUO], F32R) as w_a, \
                nc.sbuf_tensor("w_split_b", [P, NDUO - W_PART, DUO], F32R) as w_b:
            pass
        w1 = sb("w1", [P, NCH, H1])
        w2 = sb("w2", [P, K1, H2])
        w1d = sb("w1d", [ND, H1])
        w3 = sb("w3", [P, K2])
        b1 = sb("b1", [P, K1])
        b2 = sb("b2", [P, K2])
        dense = sb("dense", [P, BATCH // P, ND])
        zT = [sb(f"zT{b}", [P, NCH, BLK]) for b in range(NBLK)]
        h1T = sb("h1T", [P, 2, K1, BLK])
        h2T = sb("h2T", [P, 2, K2, BLK])
        denseT = sb("denseT", [ND, BATCH])
        y_sb = sb("y_sb", [1, BATCH])
        N_TOP_IN = 7

        def w_cols(d, a, e):
            part, d = (w_a, d) if d < W_PART else (w_b, d - W_PART)
            return part[:, :, :].rearrange("p d c -> p (d c)")[:, DUO * d + a:DUO * d + e]

        left = ps("left", [P, 2 * NLEFT, BLK])
        z_ps = ps("z_ps", [P, BLK])
        x_ps = ps("x_ps", [P, BLK])
        h1_ps, h2_ps, y_ps, d_ps = left[:, 0:2, :], left[:, 2:4, :], left[0:1, 4, :], x_ps[0:ND, :]

        ids_loaded = sem("ids_loaded")
        const_set = sem("const_set")
        consts = sem("consts")
        w_zeroed = sem("w_zeroed")
        rows_loaded = [sem(f"rows_loaded{r}") for r in range(NROWS)]
        w_loaded = [sem(f"w_loaded{r}") for r in range(NWRAW)]
        w_hi = sem("w_hi")
        w_ready = sem("w_ready")
        pairs_begun = sem("pairs_begun")
        x_in_psum = sem("x_in_psum")
        x_ready = sem("x_ready")
        x_hi = sem("x_hi")
        x_lo = sem("x_lo")
        f_ready = sem("f_ready")
        left_done = sem("left_done")
        prod_ready = sem("prod_ready")
        sum_done = sem("sum_done")
        z_copied = sem("z_copied")
        z_stored = sem("z_stored")
        w1_moved = sem("w1_moved")
        top_in = sem("top_in")
        zT_in = [sem(f"zT_in{b}") for b in range(NBLK)]
        d_in_psum = sem("d_in_psum")
        d_ready = sem("d_ready")
        h1_in_psum = sem("h1_in_psum")
        h1_ready = sem("h1_ready")
        h2_in_psum = sem("h2_in_psum")
        h2_ready = sem("h2_ready")
        y_in_psum = sem("y_in_psum")
        y_ready = sem("y_ready")
        y_out = sem("y_out")

        block = ctx.enter_context(nc.Block())

        @block.sync
        def _(sp):
            def store_z(b, c):
                sp.wait_ge(z_copied, NCH * b + c + 1)
                sp.dma_start(z_dram[b, :, c, :], z_out[:, :]).then_inc(z_stored, 16)

            for n in range(NQUAD):
                if n >= NWRAW:
                    sp.wait_ge(w_ready, n - NWRAW + 1)
                for c, p, k in quad_runs(n):
                    for half in (0, D):
                        sp.dma_start(w_raw[half:half + D, n % NWRAW, c:c + k * D].rearrange("d (p e) -> d p e", e=D),
                                     t["L0_rec_W"][p:p + k, :, :].rearrange("p d e -> d p e")).then_inc(w_loaded[n % NWRAW], 16)
                if n % QCH == 8 and n > QCH:
                    store_z(0, n // QCH - 1)
            store_z(0, NCH - 1)

            sp.wait_ge(w_zeroed, 1)
            zeros = w_cols(EMPTY[0], 0, D)[0:8, :].bitcast(F32)
            for c in range(NCH):
                for d in range(4 * QCH * c, 4 * QCH * (c + 1)):
                    _, r = z_row(d)
                    lower, upper = halves(d)
                    if lower is None:
                        sp.dma_start(w1_dram[r, c, :].rearrange("(a n) -> a n", n=D), zeros).then_inc(w1_moved, 16)
                        sp.dma_start(w1_dram[r + 1:r + 2, c, :], w_top1[upper:upper + 1, :]).then_inc(w1_moved, 16)
                    else:
                        sp.dma_start(w1_dram[r:r + 2, c, :], w_top1[lower:lower + 2, :]).then_inc(w1_moved, 16)
                store_z(1, c)
            with sp.Fori(2, NBLK - 1) as b:
                for c in range(NCH):
                    store_z(b, c)

            store_z(NBLK - 1, 0)
            sp.wait_ge(left_done, NDUO * (NBLK - 1) + W_PART)
            sp.wait_ge(w1_moved, 16 * (NDUO + len(EMPTY)))
            sp.wait_ge(z_stored, 16 * NCH * (NBLK - 1))
            sp.dma_start(w1[:, :, :], w1_dram[:, :, :]).then_inc(top_in, 16)
            sp.dma_start(w2[:, :, :], t["W_top2"].rearrange("(k p) n -> p k n", p=P)).then_inc(top_in, 16)
            sp.dma_start(w1d[:, :], w_top1[NPAIR:NPAIR + ND, :]).then_inc(top_in, 16)
            sp.dma_start(dense[:, :, :], t["dense_ctx"].rearrange("(t p) k -> p t k", p=P)).then_inc(top_in, 16)
            sp.dma_start(b1[:, :], t["b_top1"].rearrange("(k p) -> p k", p=P), allow_slow_non_contiguous=True).then_inc(top_in, 16)
            sp.dma_start(b2[:, :], t["b_top2"].rearrange("(k p) -> p k", p=P), allow_slow_non_contiguous=True).then_inc(top_in, 16)
            sp.dma_start(w3[:, :], t["W_top3"].rearrange("(k p) o -> p (k o)", p=P), allow_slow_non_contiguous=True).then_inc(top_in, 16)
            for b in range(2):
                sp.dma_start(zT[b][:, :, :], z_dram[b, :, :, :]).then_inc(zT_in[b], 16)
            for c in range(1, NCH - 1):
                store_z(NBLK - 1, c)
            sp.wait_ge(left_done, NDUO * NBLK)
            for b in range(2, NBLK - 1):
                sp.dma_start(zT[b][:, :, :], z_dram[b, :, :, :]).then_inc(zT_in[b], 16)
            store_z(NBLK - 1, NCH - 1)
            sp.wait_ge(z_stored, 16 * NCH * NBLK)
            sp.dma_start(zT[NBLK - 1][:, :, :], z_dram[NBLK - 1, :, :, :]).then_inc(zT_in[NBLK - 1], 16)
            sp.wait_ge(y_ready, NBLK)
            sp.dma_start(t["y"].rearrange("b o -> o b"), y_sb[:, :]).then_inc(y_out, 16)
            sp.wait_ge(y_out, 16)

        @block.gpsimd
        def _(pool):
            nc.gpsimd.memset(ident[:, :], 0.0).then_inc(const_set, 1)
            nc.gpsimd.memset(pick[:, :], 0.0).then_inc(const_set, 1)
            pool.wait_ge(const_set, 2)
            nc.gpsimd.affine_select(out=ident[:, :], in_=ident[:, :], compare_op=ALU.not_equal, fill=1.0,
                                    base=0, pattern=[[-1, P]], channel_multiplier=1).then_inc(consts, 1)
            pool.wait_ge(consts, 1)
            nc.gpsimd.memset(pick[0:D, 30:31], 1.0).then_inc(consts, 1)
            pool.wait_ge(consts, 2)
            nc.gpsimd.memset(pick[D:P, 31:32], 1.0).then_inc(consts, 1)
            ids = t["ids"].rearrange("(t p) f -> p t f", p=P)

            def body(b):
                for r in range(NROWS):
                    wait(pool, rows_loaded[r], 16 * 2 * TB * (NM // NROWS) * b)
                pool.dma_start(ids_now[:, :, :], ids[:, bass.ds(b * TB, TB), :]).then_inc(ids_loaded, 16)
                pool.wait_ge(ids_loaded, 16 * b + 16)
                for s in range(NM):
                    m = NM - 1 - s
                    r = s % NROWS
                    wait(pool, x_in_psum, NM * b + s - NROWS + 1)
                    pool.sem_inc(pairs_begun, 1)
                    for f in (2 * m + 1, 2 * m):
                        for k in range(TB):
                            pool.indirect_dma_start(
                                rows[:, r, k, f % 2, :], None, tables[f],
                                bass.IndirectOffsetOnAxis(ap=ids_now[:, k, f:f + 1], axis=0),
                            ).then_inc(rows_loaded[r], 16)

            body(0)
            with pool.Fori(1, NBLK) as b:
                body(b)

        @block.scalar
        def _(act):
            def split_w(n):
                loads = sum(2 * len(quad_runs(k)) for k in range(n % NWRAW, n + 1, NWRAW))
                act.wait_ge(w_loaded[n % NWRAW], 16 * loads)
                for a, e in quad_spans(n):
                    last = nc.scalar.activation(w_cols(4 * n, a, e), w_raw[:, n % NWRAW, a:e], ACT.Copy)
                last.then_inc(w_hi, 1)

            def body(b0, first, final):
                w_next = 0
                for kind, v, o in steps_of(first, final):
                    b = b0 + o
                    if first and kind == "left" and v % 4 == 0:
                        while w_next < min(NQUAD, v // 4 + W_AHEAD):
                            split_w(w_next)
                            w_next += 1
                    if kind == "x":
                        wait(act, x_in_psum, NM * b + X_COUNT[v])
                        wait(act, prod_ready, NUNIT * b - NUNIT + LAST_UNIT[v] + 1)
                        nc.scalar.activation(xT[:, v, :], x_ps[:, :], ACT.Copy).then_inc(x_ready, 1)
                        wait(act, f_ready, NGRP * b + F_COUNT.get(2 * v + 2, 0))
                        nc.scalar.activation(x_parts[:, 0, :], x_ps[:, :], ACT.Copy).then_inc(x_hi, 1)
                    if kind == "f":
                        wait(act, x_lo, NM * b + X_COUNT[v // 2])
                        ob, user = before_in_ring(SLOT, GROUPS, v)
                        wait(act, left_done, NDUO * (b + ob) + LAST[user] + 1)
                        parts = x_parts[D * (v % 2):D * (v % 2) + D, :, :]
                        nc.scalar.activation(x_twice[0:D, SLOT[v], :, :], parts, ACT.Copy)
                        nc.scalar.activation(x_twice[D:P, SLOT[v], :, :], parts, ACT.Copy).then_inc(f_ready, 1)
                    if kind == "sum" and v % QCH == QCH - 1:
                        c = v // QCH
                        wait(act, sum_done, NQUAD * b + v + 1)
                        wait(act, z_stored, 16 * (NCH * b + c))
                        nc.scalar.activation(z_out[:, :], z_ps[:, :], ACT.Copy).then_inc(z_copied, 1)

            over_blocks(act, body)

            for b in range(NBLK):
                act.wait_ge(d_in_psum, b + 1)
                nc.scalar.activation(denseT[:, b * BLK:(b + 1) * BLK], d_ps, ACT.Copy).then_inc(d_ready, 1)
            act.wait_ge(top_in, 16 * N_TOP_IN)
            for b in range(NBLK):
                for q in range(K1):
                    act.wait_ge(h1_in_psum, K1 * b + q + 1)
                    if b >= 2:
                        act.wait_ge(h2_in_psum, K2 * (b - 1))
                    nc.scalar.activation(h1T[:, b % 2, q, :], h1_ps[:, (K1 * b + q) % 2, :], ACT.Relu,
                                         bias=b1[:, q:q + 1]).then_inc(h1_ready, 1)
                for q in range(K2):
                    act.wait_ge(h2_in_psum, K2 * b + q + 1)
                    if b >= 2:
                        act.wait_ge(y_in_psum, b - 1)
                    nc.scalar.activation(h2T[:, b % 2, q, :], h2_ps[:, (K2 * b + q) % 2, :], ACT.Relu,
                                         bias=b2[:, q:q + 1]).then_inc(h2_ready, 1)
                act.wait_ge(y_in_psum, b + 1)
                nc.scalar.activation(y_sb[:, b * BLK:(b + 1) * BLK], y_ps, ACT.Copy).then_inc(y_ready, 1)

        @block.vector
        def _(dve):
            for d in EMPTY:
                last = nc.vector.memset(w_cols(d, 0, D).bitcast(F32), 0.0)
            last.then_inc(w_zeroed, 1)

            def split_w(n):
                dve.wait_ge(w_hi, n + 1)
                for a, e in quad_spans(n):
                    cols = w_cols(4 * n, a, e)[D:P, :]
                    last = nc.vector.tensor_tensor(cols, w_raw[D:P, n % NWRAW, a:e], cols, ALU.subtract)
                last.then_inc(w_ready, 1)

            def body(b0, first, final):
                w_next = 0
                for kind, v, o in steps_of(first, final):
                    b = b0 + o
                    if first and kind == "left" and v % 4 == 0:
                        while w_next < min(NQUAD, v // 4 + W_AHEAD):
                            split_w(w_next)
                            w_next += 1
                    if kind == "lo":
                        wait(dve, x_hi, NM * b + X_COUNT[v])
                        nc.vector.tensor_tensor(x_parts[:, 1, :], x_ps[:, :], x_parts[:, 0, :],
                                                ALU.subtract).then_inc(x_lo, 1)
                    if kind == "left" and v % 2 == 1:
                        u = v // 2
                        m0, m1 = DUOS[v - 1][1], DUOS[v][1]
                        wait(dve, left_done, NDUO * b + v + 1)
                        wait(dve, x_ready, NM * b + X_COUNT[min(m0, m1)])
                        wait(dve, sum_done, NQUAD * b + (u - NPROD) // 2 + 1)
                        if m0 == m1:
                            other = xT[:, m0:m0 + 1, :].to_broadcast([P, 2, BLK])
                        else:
                            step = m1 - m0
                            other = xT[:, m0:m1 + 1:step, :] if step > 0 else xT[:, m0:m1 - 1 if m1 else None:step, :]
                        nc.vector.tensor_tensor(prod[:, u % NPROD, :, :], left[:, 2 * (u % NLEFT):2 * (u % NLEFT) + 2, :],
                                                other, ALU.mult).then_inc(prod_ready, 1)

            over_blocks(dve, body)

        @block.tensor
        def _(pe):
            pe.wait_ge(consts, 3)

            def body(b0, first, final):
                for kind, v, o in steps_of(first, final):
                    b = b0 + o
                    if kind == "x":
                        s = NM - 1 - v
                        wait(pe, rows_loaded[s % NROWS], 16 * 2 * TB * (NM // NROWS * b + s // NROWS + 1))
                        wait(pe, x_ready, NM * b + X_COUNT[v] - 1)
                        wait(pe, x_lo, NM * b + X_COUNT[v] - 1)
                        for k in range(TB):
                            both = rows[:, s % NROWS, k, :, :].rearrange("p f d -> p (f d)")
                            last = nc.tensor.transpose(x_ps[:, k * P:(k + 1) * P], both, ident[:, :])
                        last.then_inc(x_in_psum, 1)
                    if kind == "left":
                        i, u = DUOS[v][0], v // 2
                        if v == FIRST[i]:
                            wait(pe, f_ready, NGRP * b + F_COUNT[i])
                        if first and v % 4 == 0:
                            pe.wait_ge(w_ready, v // 4 + 1)
                        if v % 2 == 0:
                            ob, user = before_in_ring([k % NLEFT for k in range(NUNIT)], list(range(NUNIT)), u)
                            wait(pe, prod_ready, NUNIT * (b + ob) + user + 1)
                        place = 2 * (u % NLEFT) + v % 2
                        for part in range(2):
                            last = nc.tensor.matmul(left[:, place, :], w_cols(v, 0, DUO),
                                                    x_twice[:, SLOT[i], part, :], start=part == 0, stop=part == 1)
                        last.then_inc(left_done, 1)
                    if kind == "sum":
                        wait(pe, prod_ready, NUNIT * b + 2 * v + 2)
                        k = v % QCH
                        if k == 0:
                            wait(pe, z_copied, NCH * b + v // QCH)
                        for q in range(4):
                            last = nc.tensor.matmul(z_ps[32 * q:32 * q + 32, :], pick[:, 30 - 2 * k:62 - 2 * k],
                                                    prod[:, (2 * v + q // 2) % NPROD, q % 2, :],
                                                    start=k == 0, stop=k == QCH - 1)
                        last.then_inc(sum_done, 1)

            over_blocks(pe, body)

            pe.wait_ge(top_in, 16 * N_TOP_IN)
            for b in range(NBLK):
                if b:
                    pe.wait_ge(d_ready, b)
                for k in range(TB):
                    last = nc.tensor.transpose(d_ps[:, k * P:(k + 1) * P], dense[:, TB * b + k, :], ident[:, :])
                last.then_inc(d_in_psum, 1)
            pe.wait_ge(d_ready, NBLK)
            for b in range(NBLK):
                pe.wait_ge(zT_in[b], 16)
                for q in range(K1):
                    n = K1 * b + q
                    if n >= 2:
                        pe.wait_ge(h1_ready, n - 1)
                    for c in range(NCH):
                        nc.tensor.matmul(h1_ps[:, n % 2, :], w1[:, c, q * P:(q + 1) * P], zT[b][:, c, :],
                                         start=c == 0, stop=False)
                    nc.tensor.matmul(h1_ps[:, n % 2, :], w1d[:, q * P:(q + 1) * P], denseT[:, b * BLK:(b + 1) * BLK],
                                     start=False, stop=True).then_inc(h1_in_psum, 1)
                pe.wait_ge(h1_ready, K1 * (b + 1))
                for q in range(K2):
                    n = K2 * b + q
                    if n >= 2:
                        pe.wait_ge(h2_ready, n - 1)
                    for c in range(K1):
                        last = nc.tensor.matmul(h2_ps[:, n % 2, :], w2[:, c, q * P:(q + 1) * P], h1T[:, b % 2, c, :],
                                                start=c == 0, stop=c == K1 - 1)
                    last.then_inc(h2_in_psum, 1)
                pe.wait_ge(h2_ready, K2 * (b + 1))
                if b:
                    pe.wait_ge(y_ready, b)
                for c in range(K2):
                    last = nc.tensor.matmul(y_ps, w3[:, c:c + 1], h2T[:, b % 2, c, :], start=c == 0, stop=c == K2 - 1)
                last.then_inc(y_in_psum, 1)


def kernel(**inputs):
    import concourse.bacc as bacc
    from concourse.bass_utils import run_bass_kernel_spmd

    nc = bacc.Bacc("TRN2", target_bir_lowering=False, num_devices=1)
    arrays, tensors = {}, {}
    for name, value in inputs.items():
        a = np.ascontiguousarray(value)
        arrays[f"in_{name}"] = a
        tensors[name] = nc.dram_tensor(f"in_{name}", a.shape, mybir.dt.from_np(a.dtype), kind="ExternalInput").ap()
    tensors["y"] = nc.dram_tensor("out_y", (BATCH, 1), F32, kind="ExternalOutput").ap()
    build(nc, tensors)
    result = run_bass_kernel_spmd(nc, [arrays], core_ids=[0])
    return result.results[0]["out_y"]
```

```python
from contextlib import ExitStack

import concourse.bass as bass
import concourse.mybir as mybir
import numpy as np

F32 = mybir.dt.float32
F32R = mybir.dt.float32r
I32 = mybir.dt.int32
ALU = mybir.AluOpType
ACT = mybir.ActivationFunctionType

F, D, P = 32, 64, 128
BATCH, BLK = 2048, 512
NBLK = BATCH // BLK
TB = BLK // P
DUO = 2 * D
NPAIR = F * (F - 1) // 2
NM = F // 2

GROUPS = list(range(F - 2, -1, -1))
DUOS = [(i, m) for i in GROUPS for m in sorted(range((i + 1) // 2, NM), reverse=i == 0)]
NDUO = len(DUOS)
NUNIT = NDUO // 2
NQUAD = NDUO // 4
QCH = 16
NCH = NQUAD // QCH
NGRP = len(GROUPS)
FIRST = {i: next(d for d, (g, _) in enumerate(DUOS) if g == i) for i in GROUPS}
LAST = {i: max(d for d, (g, _) in enumerate(DUOS) if g == i) for i in GROUPS}
LAST_UNIT = {m: max(d for d, (_, k) in enumerate(DUOS) if k == m) // 2 for m in range(NM)}

NROWS = 4
NWHI = 2
NWLOAD = 8
NPROD = 4
NLEFT = 3
NTWICE = 4
LAG = 4
W_AHEAD = 3
W_PER_X, W_X = 3, 6
W_EVERY = 6
W_PART = 3 * 4 * QCH
F_VECTOR = 25
W_LO_AFTER = 3
X_BEFORE = 0
LO_AFTER, TWICE_AFTER = 3, 5


def pair_index(i, j):
    return i * F - i * (i + 1) // 2 + (j - i - 1)


def halves(d):
    i, m = DUOS[d]
    return [pair_index(i, j) if j > i else None for j in (2 * m, 2 * m + 1)]


EMPTY = [d for d in range(NDUO) if halves(d)[0] is None]


def loads(n):
    runs = []
    cols = [(c, p) for c, p in enumerate(h for d in range(4 * n, 4 * n + 4) for h in halves(d)) if p is not None]
    for c, p in cols:
        if runs and runs[-1][0] + runs[-1][2] == c and runs[-1][1] + runs[-1][2] == p:
            runs[-1][2] += 1
        else:
            runs.append([c, p, 1])
    return [(c * D, p, k) for c, p, k in runs]


def spans(n):
    out = []
    for c, _, k in loads(n):
        if out and sum(out[-1]) == c:
            out[-1][1] += k * D
        else:
            out.append([c, k * D])
    return out


def w_due(kind, v, late=0):
    if kind == "x" and X_COUNT[v] <= W_X:
        return min(NQUAD, W_PER_X * X_COUNT[v])
    if kind == "left":
        v = max(v - late, 0)
        return min(NQUAD, max(v // 4 + W_AHEAD, W_PER_X * W_X + (v - W_X ** 2) // W_EVERY if v > W_X ** 2 else 0))
    return 0


def z_row(d):
    return d // (4 * QCH), 32 * (d % 4) + 2 * (d // 4 % QCH)


def twice_slots():
    slots, place = {}, 0
    skips = SKIPS[:-NGRP % NTWICE]
    for i in GROUPS:
        slots[i] = place % NTWICE
        place += 2 if i in skips else 1
    return slots


SKIPS = (8, 5)
SLOT = twice_slots()


def before_in_ring(slots, order, x):
    at = order.index(x)
    for k in range(at - 1, at - 1 - len(order), -1):
        if slots[order[k]] == slots[x]:
            return (0 if k >= 0 else -1), order[k]


AHEAD = NTWICE - 1
NEXT_X = {15: 4, 14: 6, 13: 8, 12: 10}
NEXT_F = {30: 6, 29: 8, 28: 11}
FIRST_X, START = NM - 2, 4


def block_steps(first):
    before = {d: [] for d in range(NDUO)}

    def lay_out(i, at, latest, offset):
        before[at].append(("hi", i, offset))
        before[min(at + LO_AFTER, latest)].append(("lo", i, offset))
        if i < F_VECTOR:
            before[min(at + TWICE_AFTER, latest)].append(("twice", i, offset))

    at = START if first else 0
    for i in GROUPS[AHEAD:]:
        _, user = before_in_ring(SLOT, GROUPS, i)
        last, at = at, max(at, FIRST[user - 1] if user > i else 0)
        if i % 2 == 1 and i // 2 < (FIRST_X if first else min(NEXT_X)):
            before[max(last, at - X_BEFORE)].append(("x", i // 2, 0))
        lay_out(i, at, FIRST[i], 0)
    for m, k in NEXT_X.items():
        before[FIRST[0] + k].append(("x", m, 1))
    for i, k in NEXT_F.items():
        lay_out(i, FIRST[0] + k, NDUO - 1, 1)
    steps = []
    for d in range(NDUO):
        steps += before[d] + [("left", d, 0)]
        n, rest = divmod(d - 3 - LAG, 4)
        if rest == 0:
            steps.append(("sum", n % NQUAD, 0 if n >= 0 else -1))
    return steps


def steps_of(first, last):
    steps = [s for s in block_steps(first) if not (first and s[2] < 0) and not (last and s[2] > 0)]
    if last:
        steps += [(kind, v, 0) for kind, v, o in steps if o < 0]
    if first:
        steps = [(kind, v, 0) for kind, v, o in steps if o > 0 and not (kind == "x" and v < FIRST_X)] + steps
    return steps


def w_by_chunk(c):
    due = 0
    for kind, v, _ in steps_of(True, False):
        if (kind, v) == ("sum", QCH * c + QCH - 1):
            return due
        due = max(due, w_due(kind, v))
    return NQUAD


F_COUNT = {i: F - 1 - i for i in GROUPS}
X_COUNT = {m: NM - m for m in range(NM)}
N_VECTOR = F - 1 - F_VECTOR
N_SCALAR = F_VECTOR


TOP_STEPS = [(1, 0), (1, 1), (2, 0), (1, 2), (2, 1), (1, 3), (2, 2), (2, 3)]


def own(i):
    return slice(D * (i % 2), D * (i % 2) + D)


def other(i):
    return own(i + 1)


def wait(engine, semaphore, value):
    if not isinstance(value, int) or value > 0:
        engine.wait_ge(semaphore, value)


def over_blocks(engine, body):
    body(0, True, False)
    with engine.Fori(1, NBLK - 1) as b:
        body(b, False, False)
    body(NBLK - 1, False, True)


def build(nc, t):
    H1, H2 = t["W_top2"].shape
    ND = t["dense_ctx"].shape[1]
    K1, K2 = H1 // P, H2 // P
    tables = [t[f"tbl_{f}"] for f in range(F)]
    w_top1 = t["W_top1"]
    z_dram = nc.dram_tensor("z_dram", (NBLK, P, NCH, BLK), F32, kind="Internal").ap()
    w1_dram = nc.dram_tensor("w1_dram", (P, NCH, H1), F32, kind="Internal").ap()
    dense_dram = nc.dram_tensor("dense_dram", (ND, NBLK, BLK), F32, kind="Internal").ap()
    assert ND == len(EMPTY)

    with ExitStack() as ctx:
        sb = lambda name, shape, dt=F32: ctx.enter_context(nc.sbuf_tensor(name, shape, dt))
        ps = lambda name, shape: ctx.enter_context(nc.psum_tensor(name, shape, F32))
        sem = lambda name: ctx.enter_context(nc.semaphore(name))

        ident = sb("ident", [P, P])
        pick = sb("pick", [P, 64])
        w_hi_too = sb("w_hi_too", [P, NWHI, 4 * DUO], F32R)
        xT = sb("xT", [P, NM, BLK])
        x_twice = sb("x_twice", [P, NTWICE, 2, BLK], F32R)
        rows = sb("rows", [P, NROWS, TB, 2, D])
        prod = sb("prod", [P, NPROD, 2, BLK])
        z_out = sb("z_out", [P, BLK])
        ids_now = sb("ids_now", [P, TB, F], I32)

        with nc.sbuf_tensor("w_split_a", [P, W_PART, DUO], F32R) as w_a, \
                nc.sbuf_tensor("w_split_b", [P, NDUO - W_PART, DUO], F32R) as w_b:
            pass
        with ExitStack() as places:
            w_raw = [places.enter_context(nc.sbuf_tensor(f"w_raw{n}", [P, 4 * DUO], F32)) for n in range(NQUAD)]
        w1 = sb("w1", [P, NCH, H1])
        w2 = sb("w2", [P, K1, H2])
        w3 = sb("w3", [P, K2])
        b1 = sb("b1", [P, K1])
        b2 = sb("b2", [P, K2])
        zT = sb("zT", [P, NBLK, NCH, BLK])
        h1T = sb("h1T", [P, 2, K1, BLK])
        h2T = sb("h2T", [P, NBLK, K2, BLK])
        y_sb = sb("y_sb", [P, BLK])
        N_TOP_IN = 5

        def w_cols(d, a, e):
            part, d = (w_a, d) if d < W_PART else (w_b, d - W_PART)
            return part[:, :, :].rearrange("p d c -> p (d c)")[:, DUO * d + a:DUO * d + e]

        left = ps("left", [P, 2 * NLEFT, BLK])
        z_ps = ps("z_ps", [P, BLK])
        x_ps = ps("x_ps", [P, BLK])
        h1_ps, h2_ps, y_ps = left[:, 0:2, :], left[:, 2:4, :], left[:, 4, :]
        dense = z_out[:, 0:BATCH // P * ND].rearrange("p (t k) -> p t k", k=ND)
        dense_ps = left[0:ND, 0:NBLK, :]
        denseT = prod[0:ND, 2:4, :, :].rearrange("k a b n -> k (a b) n")

        first_ids_loaded = sem("first_ids_loaded")
        ids_loaded = sem("ids_loaded")
        const_set = sem("const_set")
        consts = sem("consts")
        w_zeroed = sem("w_zeroed")
        rows_loaded = [sem(f"rows_loaded{r}") for r in range(NROWS)]
        w_loaded = [sem(f"w_loaded{r}") for r in range(NWLOAD)]
        w_hi = sem("w_hi")
        w_ready = sem("w_ready")
        pairs_begun = sem("pairs_begun")
        x_in_psum = sem("x_in_psum")
        x_ready = sem("x_ready")
        f_hi = sem("f_hi")
        f_lo = sem("f_lo")
        f_vector = sem("f_vector")
        f_scalar = sem("f_scalar")
        left_done = sem("left_done")
        prod_ready = sem("prod_ready")
        sum_done = sem("sum_done")
        z_copied = sem("z_copied")
        z_stored = sem("z_stored")
        w1_moved = sem("w1_moved")
        top_in = sem("top_in")
        zT_in = [sem(f"zT_in{b}") for b in range(NBLK)]
        dense_in = sem("dense_in")
        dense_in_psum = sem("dense_in_psum")
        denseT_ready = sem("denseT_ready")
        dense_stored = sem("dense_stored")
        dense_rows_in = [sem("dense_rows_in"), sem("last_dense_rows_in")]
        h1_in_psum = sem("h1_in_psum")
        h1_ready = sem("h1_ready")
        h2_in_psum = sem("h2_in_psum")
        h2_ready = sem("h2_ready")
        y_in_psum = sem("y_in_psum")
        y_ready = sem("y_ready")
        y_ready_too = sem("y_ready_too")
        y_out = sem("y_out")

        block = ctx.enter_context(nc.Block())

        @block.sync
        def _(sp):
            def store_z(b, c):
                sp.wait_ge(z_copied, NCH * b + c + 1)
                sp.dma_start(z_dram[b, :, c, :], z_out[:, :]).then_inc(z_stored, 16)

            sp.dma_start(ids_now[:, :, :], t["ids"].rearrange("(t p) f -> p t f", p=P)[:, 0:TB, :]).then_inc(first_ids_loaded, 16)
            sp.dma_start(dense[:, :, :], t["dense_ctx"].rearrange("(t p) k -> p t k", p=P)).then_inc(dense_in, 16)

            for n in range(NQUAD):
                if n == 2:
                    sp.wait_ge(denseT_ready, 1)
                    sp.dma_start(dense_dram[:, :, :], denseT).then_inc(dense_stored, 16)
                if n >= NWLOAD:
                    sp.wait_ge(w_hi, n - NWLOAD + 1)
                for c, p, k in loads(n):
                    for half in (0, D):
                        sp.dma_start(w_raw[n][half:half + D, c:c + k * D].rearrange("d (p e) -> d p e", e=D),
                                     t["L0_rec_W"][p:p + k, :, :].rearrange("p d e -> d p e")).then_inc(w_loaded[n % NWLOAD], 16)
                for c in range(NCH):
                    if min(NQUAD, w_by_chunk(c) + NWLOAD) == n + 1:
                        store_z(0, c)

            for c in range(NCH):
                for d in range(4 * QCH * c, 4 * QCH * (c + 1)):
                    _, r = z_row(d)
                    lower, upper = halves(d)
                    if lower is None:
                        k = NPAIR + EMPTY.index(d)
                        sp.dma_start(w1_dram[r:r + 1, c, :], w_top1[k:k + 1, :]).then_inc(w1_moved, 16)
                        sp.dma_start(w1_dram[r + 1:r + 2, c, :], w_top1[upper:upper + 1, :]).then_inc(w1_moved, 16)
                    else:
                        sp.dma_start(w1_dram[r:r + 2, c, :], w_top1[lower:lower + 2, :]).then_inc(w1_moved, 16)
                store_z(1, c)
            with sp.Fori(2, NBLK - 1) as b:
                for c in range(NCH):
                    store_z(b, c)

            for c in range(NCH - 1):
                store_z(NBLK - 1, c)
            sp.wait_ge(left_done, NDUO * (NBLK - 1) + W_PART)
            sp.wait_ge(w1_moved, 16 * (NDUO + len(EMPTY)))
            sp.wait_ge(z_stored, 16 * NCH * (NBLK - 1))
            sp.wait_ge(dense_stored, 16)
            sp.dma_start(w1[:, :, :], w1_dram[:, :, :]).then_inc(top_in, 16)
            for b in range(NBLK - 1):
                sp.dma_start(zT[:, b, :, :], z_dram[b, :, :, :]).then_inc(zT_in[b], 16)
            sp.dma_start(w2[:, :, :], t["W_top2"].rearrange("(k p) n -> p k n", p=P)).then_inc(top_in, 16)
            sp.dma_start(b1[:, :], t["b_top1"].rearrange("(k p) -> p k", p=P), allow_slow_non_contiguous=True).then_inc(top_in, 16)
            sp.dma_start(b2[:, :], t["b_top2"].rearrange("(k p) -> p k", p=P), allow_slow_non_contiguous=True).then_inc(top_in, 16)
            sp.dma_start(w3[:, :], t["W_top3"].rearrange("(k p) o -> p (k o)", p=P), allow_slow_non_contiguous=True).then_inc(top_in, 16)

            def dense_rows(b, e):
                for k, d in enumerate(EMPTY):
                    c, r = z_row(d)
                    sp.dma_start(zT[r:r + 1, b:e, c, :], dense_dram[k:k + 1, b:e, :]).then_inc(dense_rows_in[b // (NBLK - 1)], 16)

            for b in range(NBLK - 1):
                sp.wait_ge(zT_in[b], 16)
            dense_rows(0, NBLK - 1)
            store_z(NBLK - 1, NCH - 1)
            sp.wait_ge(z_stored, 16 * NCH * NBLK)
            sp.dma_start(zT[:, NBLK - 1, :, :], z_dram[NBLK - 1, :, :, :]).then_inc(zT_in[NBLK - 1], 16)
            sp.wait_ge(zT_in[NBLK - 1], 16)
            dense_rows(NBLK - 1, NBLK)
            sp.wait_ge(y_ready, NBLK // 2)
            sp.wait_ge(y_ready_too, NBLK // 2)
            sp.dma_start(t["y"].rearrange("(b n) o -> b (n o)", n=BLK), y_sb[0:P:32, :]).then_inc(y_out, 16)
            sp.wait_ge(y_out, 16)

        @block.gpsimd
        def _(pool):
            nc.gpsimd.memset(ident[:, :], 0.0).then_inc(const_set, 1)
            nc.gpsimd.memset(pick[:, :], 0.0).then_inc(const_set, 1)
            pool.wait_ge(const_set, 2)
            nc.gpsimd.affine_select(out=ident[:, :], in_=ident[:, :], compare_op=ALU.not_equal, fill=1.0,
                                    base=0, pattern=[[-1, P]], channel_multiplier=1).then_inc(consts, 1)
            pool.wait_ge(consts, 1)
            nc.gpsimd.memset(pick[0:D, 30:31], 1.0).then_inc(consts, 1)
            pool.wait_ge(consts, 2)
            nc.gpsimd.memset(pick[D:P, 31:32], 1.0).then_inc(consts, 1)
            ids = t["ids"].rearrange("(t p) f -> p t f", p=P)

            def body(b, first):
                if not first:
                    for r in range(NROWS):
                        pool.wait_ge(rows_loaded[r], 16 * 2 * TB * (NM // NROWS) * b)
                    pool.dma_start(ids_now[:, :, :], ids[:, bass.ds(b * TB, TB), :]).then_inc(ids_loaded, 16)
                    pool.wait_ge(ids_loaded, 16 * b)
                else:
                    pool.wait_ge(first_ids_loaded, 16)
                for s in range(NM):
                    m = NM - 1 - s
                    r = s % NROWS
                    wait(pool, x_in_psum, NM * b + s - NROWS + 1)
                    pool.sem_inc(pairs_begun, 1)
                    for f in (2 * m + 1, 2 * m):
                        for k in range(TB):
                            pool.indirect_dma_start(
                                rows[:, r, k, f % 2, :], None, tables[f],
                                bass.IndirectOffsetOnAxis(ap=ids_now[:, k, f:f + 1], axis=0),
                            ).then_inc(rows_loaded[r], 16)

            body(0, True)
            with pool.Fori(1, NBLK) as b:
                body(b, False)

        @block.scalar
        def _(act):
            def split_w(n):
                act.wait_ge(w_loaded[n % NWLOAD], 16 * sum(2 * len(loads(k)) for k in range(n % NWLOAD, n + 1, NWLOAD)))
                if n >= NWHI:
                    act.wait_ge(w_ready, n - NWHI + 1)
                for at, k in spans(n):
                    raw = w_raw[n][:, at:at + k]
                    nc.scalar.activation(w_hi_too[D:P, n % NWHI, at:at + k], raw[D:P, :], ACT.Copy)
                    last = nc.scalar.activation(w_cols(4 * n, at, at + k)[0:D, :], raw[0:D, :], ACT.Copy)
                last.then_inc(w_hi, 1)

            def body(b0, first, final):
                w_next = 0
                for kind, v, o in steps_of(first, final):
                    b = b0 + o
                    while first and w_next < w_due(kind, v):
                        split_w(w_next)
                        w_next += 1
                    if kind == "x":
                        wait(act, x_in_psum, NM * b + X_COUNT[v])
                        wait(act, prod_ready, NUNIT * b - NUNIT + LAST_UNIT[v] + 1)
                        nc.scalar.activation(xT[:, v, :], x_ps[:, :], ACT.Copy).then_inc(x_ready, 1)
                    if kind == "hi":
                        wait(act, x_ready, NM * b + X_COUNT[v // 2])
                        ob, user = before_in_ring(SLOT, GROUPS, v)
                        wait(act, left_done, NDUO * (b + ob) + LAST[user] + 1)
                        for half in (0, D):
                            last = nc.scalar.activation(x_twice[half:half + D, SLOT[v], 0, :],
                                                        xT[own(v), v // 2, :], ACT.Copy)
                        last.then_inc(f_hi, 1)
                    if kind == "twice":
                        wait(act, f_lo, NGRP * b + F_COUNT[v])
                        nc.scalar.activation(x_twice[other(v), SLOT[v], 1, :], x_twice[own(v), SLOT[v], 1, :],
                                             ACT.Copy).then_inc(f_scalar, 1)
                    if kind == "sum" and v % QCH == QCH - 1:
                        c = v // QCH
                        wait(act, sum_done, NQUAD * b + v + 1)
                        wait(act, z_stored, 16 * (NCH * b + c))
                        nc.scalar.activation(z_out[:, :], z_ps[:, :], ACT.Copy).then_inc(z_copied, 1)

            act.wait_ge(dense_in_psum, 1)
            nc.scalar.activation(denseT, dense_ps, ACT.Copy).then_inc(denseT_ready, 1)

            over_blocks(act, body)

            act.wait_ge(top_in, 16 * N_TOP_IN)
            for layer, b in TOP_STEPS:
                if layer == 1:
                    for q in range(K1):
                        act.wait_ge(h1_in_psum, K1 * b + q + 1)
                        if b >= 2:
                            act.wait_ge(h2_in_psum, K2 * (b - 1))
                        nc.scalar.activation(h1T[:, b % 2, q, :], h1_ps[:, (K1 * b + q) % 2, :], ACT.Relu,
                                             bias=b1[:, q:q + 1]).then_inc(h1_ready, 1)
                if layer == 2:
                    for q in range(K2):
                        act.wait_ge(h2_in_psum, K2 * b + q + 1)
                        nc.scalar.activation(h2T[:, b, q, :], h2_ps[:, (K2 * b + q) % 2, :], ACT.Relu,
                                             bias=b2[:, q:q + 1]).then_inc(h2_ready, 1)
            act.wait_ge(y_in_psum, 1)
            for b in range(NBLK // 2):
                nc.scalar.activation(y_sb[32 * b:32 * b + 1, :], y_ps[32 * b:32 * b + 1, :], ACT.Copy).then_inc(y_ready, 1)

        @block.vector
        def _(dve):
            for d in EMPTY:
                last = nc.vector.memset(w_cols(d, 0, D).bitcast(F32), 0.0)
            last.then_inc(w_zeroed, 1)

            def split_w(n):
                dve.wait_ge(w_hi, n + 1)
                for at, k in spans(n):
                    last = nc.vector.tensor_tensor(w_cols(4 * n, at, at + k)[D:P, :],
                                                   w_raw[n][D:P, at:at + k],
                                                   w_hi_too[D:P, n % NWHI, at:at + k], ALU.subtract)
                last.then_inc(w_ready, 1)

            def body(b0, first, final):
                w_next = 0
                for kind, v, o in steps_of(first, final):
                    b = b0 + o
                    while first and w_next < w_due(kind, v, W_LO_AFTER):
                        split_w(w_next)
                        w_next += 1
                    if kind == "lo":
                        wait(dve, f_hi, NGRP * b + F_COUNT[v])
                        nc.vector.tensor_tensor(x_twice[own(v), SLOT[v], 1, :], xT[own(v), v // 2, :],
                                                x_twice[own(v), SLOT[v], 0, :], ALU.subtract).then_inc(f_lo, 1)
                        if v >= F_VECTOR:
                            wait(dve, f_lo, NGRP * b + F_COUNT[v])
                            nc.vector.tensor_copy(x_twice[other(v), SLOT[v], 1, :],
                                                  x_twice[own(v), SLOT[v], 1, :]).then_inc(f_vector, 1)
                    if kind == "left" and v % 2 == 1:
                        u = v // 2
                        m0, m1 = DUOS[v - 1][1], DUOS[v][1]
                        wait(dve, left_done, NDUO * b + v + 1)
                        wait(dve, x_ready, NM * b + X_COUNT[min(m0, m1)])
                        if first and u == 2:
                            dve.wait_ge(dense_stored, 16)
                        wait(dve, sum_done, NQUAD * b + (u - NPROD) // 2 + 1)
                        if m0 == m1:
                            fields = xT[:, m0:m0 + 1, :].to_broadcast([P, 2, BLK])
                        else:
                            step = m1 - m0
                            fields = xT[:, m0:m1 + 1:step, :] if step > 0 else xT[:, m0:m1 - 1 if m1 else None:step, :]
                        nc.vector.tensor_tensor(prod[:, u % NPROD, :, :], left[:, 2 * (u % NLEFT):2 * (u % NLEFT) + 2, :],
                                                fields, ALU.mult).then_inc(prod_ready, 1)

            over_blocks(dve, body)

            dve.wait_ge(y_in_psum, 1)
            for b in range(NBLK // 2, NBLK):
                nc.vector.tensor_copy(y_sb[32 * b:32 * b + 1, :], y_ps[32 * b:32 * b + 1, :]).then_inc(y_ready_too, 1)

        @block.tensor
        def _(pe):
            pe.wait_ge(consts, 3)

            def body(b0, first, final):
                for kind, v, o in steps_of(first, final):
                    b = b0 + o
                    if kind == "x":
                        s = NM - 1 - v
                        wait(pe, rows_loaded[s % NROWS], 16 * 2 * TB * (NM // NROWS * b + s // NROWS + 1))
                        wait(pe, x_ready, NM * b + X_COUNT[v] - 1)
                        for k in range(TB):
                            both = rows[:, s % NROWS, k, :, :].rearrange("p f d -> p (f d)")
                            last = nc.tensor.transpose(x_ps[:, k * P:(k + 1) * P], both, ident[:, :])
                        last.then_inc(x_in_psum, 1)
                    if kind == "left":
                        i, u = DUOS[v][0], v // 2
                        if v == FIRST[i]:
                            if i >= F_VECTOR:
                                wait(pe, f_vector, N_VECTOR * b + F_COUNT[i])
                            else:
                                wait(pe, f_scalar, N_SCALAR * b + F_COUNT[i] - N_VECTOR)
                        if first and v % 4 == 0:
                            pe.wait_ge(w_ready, v // 4 + 1)
                        if v % 2 == 0:
                            ob, user = before_in_ring([k % NLEFT for k in range(NUNIT)], list(range(NUNIT)), u)
                            wait(pe, prod_ready, NUNIT * (b + ob) + user + 1)
                        place = 2 * (u % NLEFT) + v % 2
                        for part in range(2):
                            last = nc.tensor.matmul(left[:, place, :], w_cols(v, 0, DUO),
                                                    x_twice[:, SLOT[i], part, :], start=part == 0, stop=part == 1)
                        last.then_inc(left_done, 1)
                    if kind == "sum":
                        wait(pe, prod_ready, NUNIT * b + 2 * v + 2)
                        k = v % QCH
                        if k == 0:
                            wait(pe, z_copied, NCH * b + v // QCH)
                        for q in range(4):
                            last = nc.tensor.matmul(z_ps[32 * q:32 * q + 32, :], pick[:, 30 - 2 * k:62 - 2 * k],
                                                    prod[:, (2 * v + q // 2) % NPROD, q % 2, :],
                                                    start=k == 0, stop=k == QCH - 1)
                        last.then_inc(sum_done, 1)

            pe.wait_ge(dense_in, 16)
            for k in range(BATCH // P):
                last = nc.tensor.transpose(dense_ps[:, k // TB, k % TB * P:(k % TB + 1) * P], dense[:, k, :], ident[:, :])
            last.then_inc(dense_in_psum, 1)
            pe.wait_ge(denseT_ready, 1)

            over_blocks(pe, body)

            pe.wait_ge(top_in, 16 * N_TOP_IN)
            for layer, b in TOP_STEPS:
                if layer == 1:
                    pe.wait_ge(dense_rows_in[b // (NBLK - 1)], 16 * ND)
                    for q in range(K1):
                        n = K1 * b + q
                        if n >= 2:
                            pe.wait_ge(h1_ready, n - 1)
                        for c in range(NCH):
                            last = nc.tensor.matmul(h1_ps[:, n % 2, :], w1[:, c, q * P:(q + 1) * P], zT[:, b, c, :],
                                                    start=c == 0, stop=c == NCH - 1)
                        last.then_inc(h1_in_psum, 1)
                if layer == 2:
                    pe.wait_ge(h1_ready, K1 * (b + 1))
                    for q in range(K2):
                        n = K2 * b + q
                        if n >= 2:
                            pe.wait_ge(h2_ready, n - 1)
                        for c in range(K1):
                            last = nc.tensor.matmul(h2_ps[:, n % 2, :], w2[:, c, q * P:(q + 1) * P], h1T[:, b % 2, c, :],
                                                    start=c == 0, stop=c == K1 - 1)
                        last.then_inc(h2_in_psum, 1)
            for c in range(K2):
                pe.wait_ge(h2_ready, K2 * (NBLK - 1) + c + 1)
                for b in range(NBLK):
                    last = nc.tensor.matmul(y_ps[32 * b:32 * b + 1, :], w3[:, c:c + 1], h2T[:, b, c, :],
                                            start=c == 0, stop=c == K2 - 1)
            last.then_inc(y_in_psum, 1)


def kernel(**inputs):
    import concourse.bacc as bacc
    from concourse.bass_utils import run_bass_kernel_spmd

    nc = bacc.Bacc("TRN2", target_bir_lowering=False, num_devices=1)
    arrays, tensors = {}, {}
    for name, value in inputs.items():
        a = np.ascontiguousarray(value)
        arrays[f"in_{name}"] = a
        tensors[name] = nc.dram_tensor(f"in_{name}", a.shape, mybir.dt.from_np(a.dtype), kind="ExternalInput").ap()
    tensors["y"] = nc.dram_tensor("out_y", (BATCH, 1), F32, kind="ExternalOutput").ap()
    build(nc, tensors)
    result = run_bass_kernel_spmd(nc, [arrays], core_ids=[0])
    return result.results[0]["out_y"]
```
